# Optimizing a Trainium2 kernel written in Bass

```python
import numpy as np
import jax
import jax.numpy as jnp

def _softmax(x, axis=-1):
    return jax.nn.softmax(x, axis=axis)

def _gelu(x):
    return jax.nn.gelu(x, approximate=True)

def _silu(x):
    return jax.nn.silu(x)

def _sigmoid(x):
    return jax.nn.sigmoid(x)

def _layernorm(x, axis=-1, eps=1e-05):
    m = jnp.mean(x, axis=axis, keepdims=True)
    v = jnp.var(x, axis=axis, keepdims=True)
    return (x - m) / jnp.sqrt(v + eps)

def _scatter_add(tgt, idx, src, axis=0):
    return tgt.at[idx].add(src)

def _segment_sum(src, seg, n):
    return jax.ops.segment_sum(src, seg, n)
kernel_name = 'mk_rec_standalone_d1_rec_r8_1a82c1'

def setup_inputs(seed: int=0):
    np.random.seed(seed)
    _w = jnp.asarray

    def _rec_inputs():
        import jax
        import jax.numpy as jnp
        _rk = jax.random.key(seed)
        r_A = jax.random.uniform(jax.random.fold_in(_rk, 1), (2048, 50, 100), jnp.float32, 0.0, 1)
        r_items = jnp.stack([jax.random.randint(jax.random.fold_in(jax.random.fold_in(_rk, 2), 0), (2048,), 5, 99987, jnp.int32), jax.random.randint(jax.random.fold_in(jax.random.fold_in(_rk, 2), 1), (2048,), 57, 99995, jnp.int32), jax.random.randint(jax.random.fold_in(jax.random.fold_in(_rk, 2), 2), (2048,), 2, 12496, jnp.int32), jax.random.randint(jax.random.fold_in(jax.random.fold_in(_rk, 2), 3), (2048,), 33, 99963, jnp.int32), jax.random.randint(jax.random.fold_in(jax.random.fold_in(_rk, 2), 4), (2048,), 2, 99964, jnp.int32), jax.random.randint(jax.random.fold_in(jax.random.fold_in(_rk, 2), 5), (2048,), 2, 12497, jnp.int32), jax.random.randint(jax.random.fold_in(jax.random.fold_in(_rk, 2), 6), (2048,), 43, 12496, jnp.int32), jax.random.randint(jax.random.fold_in(jax.random.fold_in(_rk, 2), 7), (2048,), 9, 99981, jnp.int32), jax.random.randint(jax.random.fold_in(jax.random.fold_in(_rk, 2), 8), (2048,), 58, 99987, jnp.int32), jax.random.randint(jax.random.fold_in(jax.random.fold_in(_rk, 2), 9), (2048,), 10, 99973, jnp.int32), jax.random.randint(jax.random.fold_in(jax.random.fold_in(_rk, 2), 10), (2048,), 3, 99983, jnp.int32), jax.random.randint(jax.random.fold_in(jax.random.fold_in(_rk, 2), 11), (2048,), 10, 99999, jnp.int32), jax.random.randint(jax.random.fold_in(jax.random.fold_in(_rk, 2), 12), (2048,), 15, 99971, jnp.int32), jax.random.randint(jax.random.fold_in(jax.random.fold_in(_rk, 2), 13), (2048,), 14, 12497, jnp.int32), jax.random.randint(jax.random.fold_in(jax.random.fold_in(_rk, 2), 14), (2048,), 27, 99972, jnp.int32), jax.random.randint(jax.random.fold_in(jax.random.fold_in(_rk, 2), 15), (2048,), 0, 99982, jnp.int32), jax.random.randint(jax.random.fold_in(jax.random.fold_in(_rk, 2), 16), (2048,), 26, 99995, jnp.int32), jax.random.randint(jax.random.fold_in(jax.random.fold_in(_rk, 2), 17), (2048,), 41, 99982, jnp.int32), jax.random.randint(jax.random.fold_in(jax.random.fold_in(_rk, 2), 18), (2048,), 6, 99995, jnp.int32), jax.random.randint(jax.random.fold_in(jax.random.fold_in(_rk, 2), 19), (2048,), 40, 99908, jnp.int32), jax.random.randint(jax.random.fold_in(jax.random.fold_in(_rk, 2), 20), (2048,), 15, 99983, jnp.int32), jax.random.randint(jax.random.fold_in(jax.random.fold_in(_rk, 2), 21), (2048,), 5, 99951, jnp.int32), jax.random.randint(jax.random.fold_in(jax.random.fold_in(_rk, 2), 22), (2048,), 14, 99970, jnp.int32), jax.random.randint(jax.random.fold_in(jax.random.fold_in(_rk, 2), 23), (2048,), 23, 99956, jnp.int32), jax.random.randint(jax.random.fold_in(jax.random.fold_in(_rk, 2), 24), (2048,), 97, 99947, jnp.int32), jax.random.randint(jax.random.fold_in(jax.random.fold_in(_rk, 2), 25), (2048,), 10, 12498, jnp.int32), jax.random.randint(jax.random.fold_in(jax.random.fold_in(_rk, 2), 26), (2048,), 34, 99999, jnp.int32), jax.random.randint(jax.random.fold_in(jax.random.fold_in(_rk, 2), 27), (2048,), 15, 99996, jnp.int32), jax.random.randint(jax.random.fold_in(jax.random.fold_in(_rk, 2), 28), (2048,), 74, 99898, jnp.int32), jax.random.randint(jax.random.fold_in(jax.random.fold_in(_rk, 2), 29), (2048,), 27, 99994, jnp.int32), jax.random.randint(jax.random.fold_in(jax.random.fold_in(_rk, 2), 30), (2048,), 38, 99982, jnp.int32), jax.random.randint(jax.random.fold_in(jax.random.fold_in(_rk, 2), 31), (2048,), 3, 99946, jnp.int32), jax.random.randint(jax.random.fold_in(jax.random.fold_in(_rk, 2), 32), (2048,), 10, 99983, jnp.int32), jax.random.randint(jax.random.fold_in(jax.random.fold_in(_rk, 2), 33), (2048,), 7, 99985, jnp.int32), jax.random.randint(jax.random.fold_in(jax.random.fold_in(_rk, 2), 34), (2048,), 54, 99973, jnp.int32), jax.random.randint(jax.random.fold_in(jax.random.fold_in(_rk, 2), 35), (2048,), 2, 99989, jnp.int32), jax.random.randint(jax.random.fold_in(jax.random.fold_in(_rk, 2), 36), (2048,), 1, 99980, jnp.int32), jax.random.randint(jax.random.fold_in(jax.random.fold_in(_rk, 2), 37), (2048,), 12, 99964, jnp.int32), jax.random.randint(jax.random.fold_in(jax.random.fold_in(_rk, 2), 38), (2048,), 37, 99999, jnp.int32), jax.random.randint(jax.random.fold_in(jax.random.fold_in(_rk, 2), 39), (2048,), 23, 99988, jnp.int32), jax.random.randint(jax.random.fold_in(jax.random.fold_in(_rk, 2), 40), (2048,), 1, 12496, jnp.int32), jax.random.randint(jax.random.fold_in(jax.random.fold_in(_rk, 2), 41), (2048,), 42, 99969, jnp.int32), jax.random.randint(jax.random.fold_in(jax.random.fold_in(_rk, 2), 42), (2048,), 37, 99997, jnp.int32), jax.random.randint(jax.random.fold_in(jax.random.fold_in(_rk, 2), 43), (2048,), 18, 99979, jnp.int32), jax.random.randint(jax.random.fold_in(jax.random.fold_in(_rk, 2), 44), (2048,), 50, 99933, jnp.int32), jax.random.randint(jax.random.fold_in(jax.random.fold_in(_rk, 2), 45), (2048,), 19, 12498, jnp.int32), jax.random.randint(jax.random.fold_in(jax.random.fold_in(_rk, 2), 46), (2048,), 0, 99994, jnp.int32), jax.random.randint(jax.random.fold_in(jax.random.fold_in(_rk, 2), 47), (2048,), 76, 99953, jnp.int32), jax.random.randint(jax.random.fold_in(jax.random.fold_in(_rk, 2), 48), (2048,), 14, 99981, jnp.int32), jax.random.randint(jax.random.fold_in(jax.random.fold_in(_rk, 2), 49), (2048,), 27, 99945, jnp.int32)], axis=1)
        return (r_A, r_items)
    r_A, r_items = _rec_inputs()

    def _L0_rec_setup():
        import jax, jax.numpy as jnp
        import numpy as np
        B, N, H, V = (512, 50, 128, 12500)
        STEP = 1

        def _gnn_cell(A, hidden, w_in, b_in, w_out, b_out, w_ih, w_hh, b_ih, b_hh, b_iah, b_oah):
            n = A.shape[1]
            input_in = jnp.matmul(A[:, :, :n], hidden @ w_in.T + b_in) + b_iah
            input_out = jnp.matmul(A[:, :, n:], hidden @ w_out.T + b_out) + b_oah
            inputs = jnp.concatenate([input_in, input_out], axis=2)
            gi = inputs @ w_ih.T + b_ih
            gh = hidden @ w_hh.T + b_hh
            i_r, i_i, i_n = jnp.split(gi, 3, axis=2)
            h_r, h_i, h_n = jnp.split(gh, 3, axis=2)
            resetgate = jax.nn.sigmoid(i_r + h_r)
            inputgate = jax.nn.sigmoid(i_i + h_i)
            newgate = jnp.tanh(i_n + resetgate * h_n)
            return newgate + inputgate * (hidden - newgate)
        key = jax.random.key(seed)
        ks = jax.random.split(key, 14)
        stdv = 1.0 / np.sqrt(H)

        def u(k, shape):
            return jax.random.uniform(k, shape, jnp.float32, -stdv, stdv)
        items = jax.random.randint(ks[0], (B, N), 0, V + 1)
        A = jax.random.uniform(ks[1], (B, N, 2 * N), jnp.float32)
        return {'items': items, 'A': A, 'emb': u(ks[2], (V + 1, H)), 'w_in': u(ks[3], (H, H)), 'b_in': u(ks[4], (H,)), 'w_out': u(ks[5], (H, H)), 'b_out': u(ks[6], (H,)), 'w_ih': u(ks[7], (3 * H, 2 * H)), 'w_hh': u(ks[8], (3 * H, H)), 'b_ih': u(ks[9], (3 * H,)), 'b_hh': u(ks[10], (3 * H,)), 'b_iah': u(ks[11], (H,)), 'b_oah': u(ks[12], (H,))}
    _L0_rec_all = _L0_rec_setup()
    _L0_rec_in = {k: v for k, v in _L0_rec_all.items() if k in ('emb', 'w_in', 'b_in', 'w_out', 'b_out', 'w_ih', 'w_hh', 'b_ih', 'b_hh', 'b_iah', 'b_oah')}
    del _L0_rec_all
    return {'r_A': r_A, 'r_items': r_items, 'L0_rec_emb': _L0_rec_in['emb'], 'L0_rec_w_in': _L0_rec_in['w_in'], 'L0_rec_b_in': _L0_rec_in['b_in'], 'L0_rec_w_out': _L0_rec_in['w_out'], 'L0_rec_b_out': _L0_rec_in['b_out'], 'L0_rec_w_ih': _L0_rec_in['w_ih'], 'L0_rec_w_hh': _L0_rec_in['w_hh'], 'L0_rec_b_ih': _L0_rec_in['b_ih'], 'L0_rec_b_hh': _L0_rec_in['b_hh'], 'L0_rec_b_iah': _L0_rec_in['b_iah'], 'L0_rec_b_oah': _L0_rec_in['b_oah']}

def reference(r_A, r_items, L0_rec_emb, L0_rec_w_in, L0_rec_b_in, L0_rec_w_out, L0_rec_b_out, L0_rec_w_ih, L0_rec_w_hh, L0_rec_b_ih, L0_rec_b_hh, L0_rec_b_iah, L0_rec_b_oah):
    import jax
    import jax.numpy as jnp

    def _L0_rec_ref(items, A, emb, w_in, b_in, w_out, b_out, w_ih, w_hh, b_ih, b_hh, b_iah, b_oah):
        import jax, jax.numpy as jnp
        import numpy as np
        B, N, H, V = (512, 50, 128, 12500)
        STEP = 1

        def _gnn_cell(A, hidden, w_in, b_in, w_out, b_out, w_ih, w_hh, b_ih, b_hh, b_iah, b_oah):
            n = A.shape[1]
            input_in = jnp.matmul(A[:, :, :n], hidden @ w_in.T + b_in) + b_iah
            input_out = jnp.matmul(A[:, :, n:], hidden @ w_out.T + b_out) + b_oah
            inputs = jnp.concatenate([input_in, input_out], axis=2)
            gi = inputs @ w_ih.T + b_ih
            gh = hidden @ w_hh.T + b_hh
            i_r, i_i, i_n = jnp.split(gi, 3, axis=2)
            h_r, h_i, h_n = jnp.split(gh, 3, axis=2)
            resetgate = jax.nn.sigmoid(i_r + h_r)
            inputgate = jax.nn.sigmoid(i_i + h_i)
            newgate = jnp.tanh(i_n + resetgate * h_n)
            return newgate + inputgate * (hidden - newgate)
        hidden = emb[items]
        for _ in range(STEP):
            hidden = _gnn_cell(A, hidden, w_in, b_in, w_out, b_out, w_ih, w_hh, b_ih, b_hh, b_iah, b_oah)
        return hidden
    y = _L0_rec_ref(r_items, r_A, L0_rec_emb, L0_rec_w_in, L0_rec_b_in, L0_rec_w_out, L0_rec_b_out, L0_rec_w_ih, L0_rec_w_hh, L0_rec_b_ih, L0_rec_b_hh, L0_rec_b_iah, L0_rec_b_oah)
    return y

_drawn_inputs = setup_inputs


def setup_inputs(seed=0):
    import zlib

    import numpy as np

    out = dict(_drawn_inputs(seed))
    spreads = {}
    factors = {'L0_rec_w_hh': 2.914}
    for name, (base, spread) in spreads.items():
        noise = np.random.default_rng([zlib.crc32(name.encode()), seed]).standard_normal(out[name].shape)
        drawn = base * np.exp(spread * noise) if base else spread * noise
        out[name] = jnp.asarray(drawn.astype(out[name].dtype))
    for name, factor in factors.items():
        out[name] = (out[name] * factor).astype(out[name].dtype)
    return out
```

```python
from contextlib import ExitStack

import concourse.bass as bass
from concourse import mybir

GRAPHS, NODES, HIDDEN, VOCAB = 2048, 50, 128, 12501
GATES = 3
PAIR = 2 * NODES
PAIRS_PER_CHUNK = 4
CHUNK = PAIRS_PER_CHUNK * PAIR
CHUNKS = GRAPHS * NODES // CHUNK
SLOTS = 2
SIDE = PAIRS_PER_CHUNK * 2 * NODES

ROW = 3 * HIDDEN
TABLE_TILE = 256
TABLE_SLOTS = 7
TABLE_TILES = -(-VOCAB // TABLE_TILE)
TABLE_ROWS = TABLE_TILES * TABLE_TILE
assert TABLE_TILES % TABLE_SLOTS == 0 and CHUNKS % SLOTS == 0

B_IAH, B_OAH, B_IH, B_HH, N_BIASES = 0, 1, 2, 5, 8


def is_first(r):
    return isinstance(r, int) and r == 0


def over_rounds(engine, rounds, slots, step):
    for s in range(slots):
        step(0, s)
    with engine.Fori(1, rounds - 1) as i:
        for s in range(slots):
            step(i, s)
    for s in range(slots):
        step(rounds - 1, s)


def later(r, s, ahead, slots):
    return r + (s + ahead) // slots, (s + ahead) % slots


def build(nc, adjacency, items, emb, w_io, w_ih, w_hh, b_io, biases, identity, out):
    f32, f32r, i32 = mybir.dt.float32, mybir.dt.float32r, mybir.dt.int32
    ALU, ACT = mybir.AluOpType, mybir.ActivationFunctionType

    with ExitStack() as ctx:
        def sbuf(name, shape, dtype=f32):
            return ctx.enter_context(nc.sbuf_tensor(name, shape, dtype))

        def psum(name):
            return ctx.enter_context(nc.psum_tensor(name, [128, 512], f32))

        def sem(name):
            return ctx.enter_context(nc.semaphore(name))

        table = nc.dram_tensor("table", [TABLE_ROWS, ROW], f32, kind="Internal").ap()

        ident = sbuf("ident", [128, 128])
        w_io_sb = sbuf("w_io_sb", [HIDDEN, 2 * HIDDEN])
        b_io_sb = sbuf("b_io_sb", [128, 2, 2 * HIDDEN])
        w_all = sbuf("w_all", [HIDDEN, 3, GATES * HIDDEN])
        w_high = sbuf("w_high", [HIDDEN, 3, GATES * HIDDEN], f32r)
        w_low = sbuf("w_low", [HIDDEN, 3, GATES * HIDDEN], f32r)
        bias = sbuf("bias", [128, N_BIASES])
        bias_ri = sbuf("bias_ri", [128, 2])
        n_pairs = GRAPHS // 2
        item = sbuf("item", [PAIR, n_pairs], i32)
        wrapped = sbuf("wrapped", [PAIR, n_pairs])
        clamped = sbuf("clamped", [PAIR, n_pairs])
        index = sbuf("index", [PAIR, n_pairs], i32)
        chunk_index = sbuf("chunk_index", [PAIR, SLOTS, PAIRS_PER_CHUNK], i32)
        row_tile = sbuf("row_tile", [128, TABLE_SLOTS, 2, ROW])
        emb_t = sbuf("emb_t", [HIDDEN, TABLE_SLOTS, 2, 128])
        rows = sbuf("rows", [PAIR, SLOTS, PAIRS_PER_CHUNK, ROW])
        adj = sbuf("adj", [PAIR, SLOTS, 2, SIDE])
        x_high = sbuf("x_high", [HIDDEN, SLOTS, 3, CHUNK], f32r)
        x_low = sbuf("x_low", [HIDDEN, SLOTS, 3, CHUNK], f32r)
        hidden_t = sbuf("hidden_t", [HIDDEN, SLOTS, CHUNK])
        reset = sbuf("reset", [HIDDEN, SLOTS, CHUNK])
        inputg = sbuf("inputg", [HIDDEN, SLOTS, CHUNK])
        gated = sbuf("gated", [HIDDEN, SLOTS, CHUNK])
        new_arg = sbuf("new_arg", [HIDDEN, SLOTS, CHUNK])
        newg = sbuf("newg", [HIDDEN, SLOTS, CHUNK])
        diff = sbuf("diff", [HIDDEN, SLOTS, CHUNK])
        scaled = sbuf("scaled", [HIDDEN, SLOTS, CHUNK])
        result = sbuf("result", [HIDDEN, SLOTS, CHUNK])

        banks = [psum(f"bank{n}") for n in range(TABLE_SLOTS)]
        agg_in, agg_out, hid_ps, reset_ps, input_ps, hidnew_ps, new_ps = banks

        consts_loaded = sem("consts_loaded")
        emb_loaded = [sem(f"emb_loaded{s}") for s in range(TABLE_SLOTS)]
        emb_transposed = sem("emb_transposed")
        emb_t_copied = sem("emb_t_copied")
        linear_done = sem("linear_done")
        row_ready = sem("row_ready")
        row_stored = [sem(f"row_stored{s}") for s in range(TABLE_SLOTS)]
        wrap_ready = sem("wrap_ready")
        clamp_ready = sem("clamp_ready")
        index_ready = sem("index_ready")
        chunk_index_ready = sem("chunk_index_ready")
        gathers_begun = sem("gathers_begun")
        adj_zeroed = sem("adj_zeroed")
        w_high_ready = sem("w_high_ready")
        w_ready = sem("w_ready")
        bias_ready = sem("bias_ready")
        rows_loaded = [sem(f"rows_loaded{s}") for s in range(SLOTS)]
        adj_loaded = [sem(f"adj_loaded{s}") for s in range(SLOTS)]
        in_aggregated = sem("in_aggregated")
        out_aggregated = sem("out_aggregated")
        hidden_turned = sem("hidden_turned")
        in_high_ready = sem("in_high_ready")
        out_high_ready = sem("out_high_ready")
        hidden_copied = sem("hidden_copied")
        hidden_high_ready = sem("hidden_high_ready")
        split_done = sem("split_done")
        reset_summed = sem("reset_summed")
        input_summed = sem("input_summed")
        hidnew_summed = sem("hidnew_summed")
        new_summed = sem("new_summed")
        reset_ready = sem("reset_ready")
        input_ready = sem("input_ready")
        gated_ready = sem("gated_ready")
        new_arg_ready = sem("new_arg_ready")
        new_ready = sem("new_ready")
        diff_ready = sem("diff_ready")
        scaled_ready = sem("scaled_ready")
        result_ready = sem("result_ready")
        result_stored = [sem(f"result_stored{s}") for s in range(SLOTS)]

        TABLE_ROUNDS = TABLE_TILES // TABLE_SLOTS
        ROUNDS = CHUNKS // SLOTS
        LOADS_AHEAD = 4
        N_CONSTS = 9

        emb_v = emb.rearrange("(t p r) h -> t p r h", p=128, r=2)
        table_v = table.rearrange("(t p r) h -> t p r h", p=128, r=2)

        block = ctx.enter_context(nc.Block())

        @block.sync
        def _(sp):
            sp.dma_start(ident[:, :], identity).then_inc(consts_loaded, 16)
            sp.dma_start(w_io_sb[:, :], w_io).then_inc(consts_loaded, 16)
            for n in range(2):
                sp.dma_start(b_io_sb[:, n, :], b_io.partition_broadcast(128)).then_inc(consts_loaded, 16)
            sp.dma_start(bias[:, :], biases).then_inc(consts_loaded, 16)
            for n in range(2):
                sp.dma_start(w_all[:, n, :], w_ih[n, :, :]).then_inc(consts_loaded, 16)
            sp.dma_start(w_all[:, 2, :], w_hh).then_inc(consts_loaded, 16)
            sp.dma_start(item[:, :], items).then_inc(consts_loaded, 16)

            def load_emb(r, s):
                if not is_first(r):
                    sp.wait_ge(row_stored[s], 16 * r)
                sp.dma_start(row_tile[:, s, :, 2 * HIDDEN:ROW],
                             emb_v[r * TABLE_SLOTS + s]).then_inc(emb_loaded[s], 16)

            for s in range(LOADS_AHEAD):
                load_emb(0, s)

            def table_step(r, s):
                sp.wait_ge(row_ready, r * TABLE_SLOTS + s + 1)
                sp.dma_start(table_v[r * TABLE_SLOTS + s], row_tile[:, s, :, :]).then_inc(row_stored[s], 16)
                ahead = later(r, s, LOADS_AHEAD, TABLE_SLOTS)
                if not (isinstance(r, int) and ahead[0] >= TABLE_ROUNDS):
                    load_emb(*ahead)

            over_rounds(sp, TABLE_ROUNDS, TABLE_SLOTS, table_step)

            def load_adj(r, s):
                for g in range(2):
                    sp.dma_start(adj[g * NODES:(g + 1) * NODES, s, g, :],
                                 adjacency[r * SLOTS + s, g]).then_inc(adj_loaded[s], 16)

            sp.wait_ge(adj_zeroed, 1)
            for s in range(SLOTS):
                load_adj(0, s)

            def step(r, s):
                if not (isinstance(r, int) and r == ROUNDS - 1):
                    sp.wait_ge(out_aggregated, r * SLOTS + s + 1)
                    load_adj(r + 1, s)
                sp.wait_ge(result_ready, r * SLOTS + s + 1)
                sp.dma_start(out[r * SLOTS + s], result[:, s, :]).then_inc(result_stored[s], 16)

            over_rounds(sp, ROUNDS, SLOTS, step)
            for s in range(SLOTS):
                sp.wait_ge(result_stored[s], 16 * ROUNDS)

        @block.gpsimd
        def _(pool):
            pool.memset(adj[:, :, :, :], 0.0).then_inc(adj_zeroed, 1)
            pool.wait_ge(index_ready, 1)
            for s in range(TABLE_SLOTS):
                pool.wait_ge(row_stored[s], 16 * TABLE_ROUNDS)

            def step(r, s):
                t = r * SLOTS + s
                if not is_first(r):
                    pool.wait_ge(hidden_turned, t - SLOTS + 1)
                pool.tensor_copy(chunk_index[:, s, :], index[:, bass.ds(t * PAIRS_PER_CHUNK, PAIRS_PER_CHUNK)])\
                    .then_inc(chunk_index_ready, 1)
                pool.wait_ge(chunk_index_ready, t + 1)
                pool.sem_inc(gathers_begun, 1)
                for q in range(PAIRS_PER_CHUNK):
                    pool.indirect_dma_start(
                        out=rows[:, s, q, :], out_offset=None, in_=table,
                        in_offset=bass.IndirectOffsetOnAxis(ap=chunk_index[:, s, q:q + 1], axis=0),
                    ).then_inc(rows_loaded[s], 16)

            over_rounds(pool, ROUNDS, SLOTS, step)

        @block.tensor
        def _(pe):
            pe.wait_ge(consts_loaded, 16 * N_CONSTS)

            def linear(r, s):
                pe.wait_ge(emb_t_copied, r * TABLE_SLOTS + s + 1)
                for n in range(2):
                    last = nc.tensor.matmul(banks[s][:, n * 2 * HIDDEN:(n + 1) * 2 * HIDDEN],
                                            emb_t[:, s, n, :], w_io_sb[:, :], start=True, stop=True)
                last.then_inc(linear_done, 1)

            def table_step(r, s):
                t = r * TABLE_SLOTS + s
                pe.wait_ge(emb_loaded[s], 16 * (r + 1))
                if not is_first(r):
                    pe.wait_ge(row_ready, t - TABLE_SLOTS + 1)
                for n in range(2):
                    last = nc.tensor.transpose(banks[s][:, n * 128:(n + 1) * 128],
                                               row_tile[:, s, n, 2 * HIDDEN:ROW], ident[:, :])
                last.then_inc(emb_transposed, 1)
                if s > 0:
                    linear(r, s - 1)
                elif not is_first(r):
                    linear(r - 1, TABLE_SLOTS - 1)

            over_rounds(pe, TABLE_ROUNDS, TABLE_SLOTS, table_step)
            linear(TABLE_ROUNDS - 1, TABLE_SLOTS - 1)

            pe.wait_ge(row_ready, TABLE_TILES)
            pe.wait_ge(w_ready, 3)

            def aggregate(r, s):
                t = r * SLOTS + s
                pe.wait_ge(rows_loaded[s], 16 * PAIRS_PER_CHUNK * (r + 1))
                pe.wait_ge(adj_loaded[s], 32 * (r + 1))
                if not (isinstance(t, int) and t == 0):
                    pe.wait_ge(split_done, 3 * t)
                for n, (bank, done) in enumerate(((agg_in, in_aggregated), (agg_out, out_aggregated))):
                    for q in range(PAIRS_PER_CHUNK):
                        at = (2 * q + n) * NODES
                        last = nc.tensor.matmul(bank[:, q * PAIR:(q + 1) * PAIR],
                                                rows[:, s, q, n * HIDDEN:(n + 1) * HIDDEN],
                                                adj[:, s, :, at:at + NODES], start=True, stop=True)
                    last.then_inc(done, 1)
                for q in range(PAIRS_PER_CHUNK):
                    last = nc.tensor.transpose(hid_ps[:, q * PAIR:(q + 1) * PAIR],
                                               rows[:, s, q, 2 * HIDDEN:ROW], ident[0:PAIR, 0:PAIR])
                last.then_inc(hidden_turned, 1)

            def gate_sum(bank, gate, sources, s, done):
                cols = slice(gate * HIDDEN, (gate + 1) * HIDDEN)
                terms = [(w, x, n) for n in sources
                         for w, x in ((w_high, x_high), (w_high, x_low), (w_low, x_high))]
                for k, (w, x, n) in enumerate(terms):
                    last = nc.tensor.matmul(bank[:, 0:CHUNK], w[:, n, cols], x[:, s, n, :],
                                            start=(k == 0), stop=(k == len(terms) - 1))
                last.then_inc(done, 1)

            aggregate(0, 0)

            def step(r, s):
                t = r * SLOTS + s
                ahead = later(r, s, 1, SLOTS)
                if isinstance(r, int) and ahead[0] >= ROUNDS:
                    pe.wait_ge(split_done, 3 * CHUNKS)
                else:
                    aggregate(*ahead)
                first = isinstance(t, int) and t == 0
                if not first:
                    pe.wait_ge(reset_ready, t)
                gate_sum(reset_ps, 0, (0, 1, 2), s, reset_summed)
                if not first:
                    pe.wait_ge(input_ready, t)
                gate_sum(input_ps, 1, (0, 1, 2), s, input_summed)
                if not first:
                    pe.wait_ge(gated_ready, t)
                gate_sum(hidnew_ps, 2, (2,), s, hidnew_summed)
                if not first:
                    pe.wait_ge(new_arg_ready, t)
                gate_sum(new_ps, 2, (0, 1), s, new_summed)

            over_rounds(pe, ROUNDS, SLOTS, step)

        @block.scalar
        def _(act):
            act.wait_ge(consts_loaded, 16 * N_CONSTS)
            for n in range(3):
                nc.scalar.activation(w_high[:, n, :], w_all[:, n, :], ACT.Copy).then_inc(w_high_ready, 1)

            def table_step(r, s):
                act.wait_ge(emb_transposed, r * TABLE_SLOTS + s + 1)
                nc.scalar.activation(emb_t[:, s, :, :], banks[s][:, 0:256].rearrange("p (r v) -> p r v", r=2),
                                     ACT.Copy).then_inc(emb_t_copied, 1)

            over_rounds(act, TABLE_ROUNDS, TABLE_SLOTS, table_step)
            act.wait_ge(bias_ready, 1)

            def split(r, s):
                t = r * SLOTS + s
                for n, (bank, done, ready, b) in enumerate((
                        (agg_in, in_aggregated, in_high_ready, B_IAH),
                        (agg_out, out_aggregated, out_high_ready, B_OAH))):
                    act.wait_ge(done, t + 1)
                    nc.scalar.activation(x_high[:, s, n, :], bank[:, 0:CHUNK], ACT.Identity,
                                         bias=bias[:, b:b + 1]).then_inc(ready, 1)
                act.wait_ge(hidden_turned, t + 1)
                if not is_first(r):
                    act.wait_ge(result_ready, t - SLOTS + 1)
                nc.scalar.activation(hidden_t[:, s, :], hid_ps[:, 0:CHUNK], ACT.Copy).then_inc(hidden_copied, 1)

            split(0, 0)

            def step(r, s):
                t = r * SLOTS + s
                ahead = later(r, s, 1, SLOTS)
                if not (isinstance(r, int) and ahead[0] >= ROUNDS):
                    split(*ahead)
                act.wait_ge(reset_summed, t + 1)
                if not is_first(r):
                    act.wait_ge(result_ready, t - SLOTS + 1)
                nc.scalar.activation(reset[:, s, :], reset_ps[:, 0:CHUNK], ACT.Sigmoid,
                                     bias=bias_ri[:, 0:1]).then_inc(reset_ready, 1)
                act.wait_ge(input_summed, t + 1)
                nc.scalar.activation(inputg[:, s, :], input_ps[:, 0:CHUNK], ACT.Sigmoid,
                                     bias=bias_ri[:, 1:2]).then_inc(input_ready, 1)
                act.wait_ge(new_arg_ready, t + 1)
                nc.scalar.activation(newg[:, s, :], new_arg[:, s, :], ACT.Tanh,
                                     bias=bias[:, B_IH + 2:B_IH + 3]).then_inc(new_ready, 1)

            over_rounds(act, ROUNDS, SLOTS, step)

        @block.vector
        def _(dve):
            dve.wait_ge(consts_loaded, 16 * N_CONSTS)
            nc.vector.tensor_tensor(bias_ri[:, :], bias[:, B_IH:B_IH + 2], bias[:, B_HH:B_HH + 2], ALU.add)\
                .then_inc(bias_ready, 1)
            nc.vector.tensor_scalar(wrapped[:, :], item[:, :], 0.0, float(VOCAB), ALU.is_lt, ALU.mult)\
                .then_inc(wrap_ready, 1)
            dve.wait_ge(wrap_ready, 1)
            nc.vector.scalar_tensor_tensor(clamped[:, :], item[:, :], float(VOCAB - 1), wrapped[:, :],
                                           ALU.min, ALU.add).then_inc(clamp_ready, 1)
            dve.wait_ge(clamp_ready, 1)
            nc.vector.tensor_scalar(index[:, :], clamped[:, :], 0.0, None, ALU.max).then_inc(index_ready, 1)
            for n in range(3):
                dve.wait_ge(w_high_ready, n + 1)
                nc.vector.tensor_tensor(w_low[:, n, :], w_all[:, n, :], w_high[:, n, :].bitcast(f32),
                                        ALU.subtract).then_inc(w_ready, 1)

            def table_step(r, s):
                dve.wait_ge(linear_done, r * TABLE_SLOTS + s + 1)
                nc.vector.tensor_tensor(row_tile[:, s, :, 0:2 * HIDDEN],
                                        banks[s][:, :].rearrange("p (r c) -> p r c", r=2),
                                        b_io_sb[:, :, :], ALU.add).then_inc(row_ready, 1)

            over_rounds(dve, TABLE_ROUNDS, TABLE_SLOTS, table_step)

            def split(r, s):
                t = r * SLOTS + s
                for n, (bank, ready, b) in enumerate(((agg_in, in_high_ready, B_IAH),
                                                      (agg_out, out_high_ready, B_OAH))):
                    dve.wait_ge(ready, t + 1)
                    nc.vector.scalar_tensor_tensor(x_low[:, s, n, :], bank[:, 0:CHUNK], bias[:, b:b + 1],
                                                   x_high[:, s, n, :].bitcast(f32), ALU.add, ALU.subtract)\
                        .then_inc(split_done, 1)
                dve.wait_ge(hidden_copied, t + 1)
                nc.vector.tensor_copy(x_high[:, s, 2, :], hidden_t[:, s, :]).then_inc(hidden_high_ready, 1)
                dve.wait_ge(hidden_high_ready, t + 1)
                nc.vector.tensor_tensor(x_low[:, s, 2, :], hidden_t[:, s, :], x_high[:, s, 2, :].bitcast(f32),
                                        ALU.subtract).then_inc(split_done, 1)

            split(0, 0)

            def step(r, s):
                t = r * SLOTS + s
                ahead = later(r, s, 1, SLOTS)
                if not (isinstance(r, int) and ahead[0] >= ROUNDS):
                    split(*ahead)
                dve.wait_ge(reset_ready, t + 1)
                dve.wait_ge(hidnew_summed, t + 1)
                nc.vector.scalar_tensor_tensor(gated[:, s, :], hidnew_ps[:, 0:CHUNK],
                                               bias[:, B_HH + 2:B_HH + 3], reset[:, s, :],
                                               ALU.add, ALU.mult).then_inc(gated_ready, 1)
                dve.wait_ge(new_summed, t + 1)
                dve.wait_ge(gated_ready, t + 1)
                nc.vector.tensor_tensor(new_arg[:, s, :], new_ps[:, 0:CHUNK], gated[:, s, :], ALU.add)\
                    .then_inc(new_arg_ready, 1)
                dve.wait_ge(new_ready, t + 1)
                nc.vector.tensor_tensor(diff[:, s, :], hidden_t[:, s, :], newg[:, s, :], ALU.subtract)\
                    .then_inc(diff_ready, 1)
                dve.wait_ge(diff_ready, t + 1)
                dve.wait_ge(input_ready, t + 1)
                nc.vector.tensor_tensor(scaled[:, s, :], diff[:, s, :], inputg[:, s, :], ALU.mult)\
                    .then_inc(scaled_ready, 1)
                dve.wait_ge(scaled_ready, t + 1)
                if not is_first(r):
                    dve.wait_ge(result_stored[s], 16 * r)
                nc.vector.tensor_tensor(result[:, s, :], scaled[:, s, :], newg[:, s, :], ALU.add)\
                    .then_inc(result_ready, 1)

            over_rounds(dve, ROUNDS, SLOTS, step)


def kernel(r_A, r_items, L0_rec_emb, L0_rec_w_in, L0_rec_b_in, L0_rec_w_out, L0_rec_b_out, L0_rec_w_ih,
           L0_rec_w_hh, L0_rec_b_ih, L0_rec_b_hh, L0_rec_b_iah, L0_rec_b_oah):
    import numpy as np
    import concourse.bacc as bacc
    from concourse.bass_utils import run_bass_kernel_spmd

    adjacency = np.asarray(r_A).reshape(CHUNKS, PAIRS_PER_CHUNK, 2, NODES, 2, NODES).transpose(0, 2, 5, 1, 4, 3)
    emb = np.zeros((TABLE_ROWS, HIDDEN), np.float32)
    emb[:VOCAB] = np.asarray(L0_rec_emb)
    arrays = {
        "adjacency": adjacency.reshape(CHUNKS, 2, NODES, SIDE),
        "items": np.asarray(r_items).reshape(GRAPHS // 2, PAIR).T,
        "emb": emb,
        "w_io": np.concatenate([np.asarray(L0_rec_w_in).T, np.asarray(L0_rec_w_out).T], axis=1),
        "w_ih": np.asarray(L0_rec_w_ih).T.reshape(2, HIDDEN, GATES * HIDDEN),
        "w_hh": np.asarray(L0_rec_w_hh).T,
        "b_io": np.concatenate([np.asarray(L0_rec_b_in), np.asarray(L0_rec_b_out)]),
        "biases": np.concatenate([np.asarray(L0_rec_b_iah)[None], np.asarray(L0_rec_b_oah)[None],
                                  np.asarray(L0_rec_b_ih).reshape(GATES, HIDDEN),
                                  np.asarray(L0_rec_b_hh).reshape(GATES, HIDDEN)]).T,
        "identity": np.eye(128, dtype=np.float32),
    }
    arrays = {name: np.ascontiguousarray(a) for name, a in arrays.items()}
    nc = bacc.Bacc("TRN2", target_bir_lowering=False, num_devices=1)
    aps = [nc.dram_tensor(name, a.shape, mybir.dt.from_np(a.dtype), kind="ExternalInput").ap()
           for name, a in arrays.items()]
    out = nc.dram_tensor("out", (CHUNKS, HIDDEN, CHUNK), mybir.dt.float32, kind="ExternalOutput").ap()
    build(nc, *aps, out)
    result = run_bass_kernel_spmd(nc, [arrays], core_ids=[0]).results[0]["out"]
    return np.ascontiguousarray(np.asarray(result).transpose(0, 2, 1)).reshape(GRAPHS, NODES, HIDDEN)
```

```python
from contextlib import ExitStack

import concourse.bass as bass
from concourse import mybir

GRAPHS, NODES, HIDDEN, VOCAB = 2048, 50, 128, 12501
GATES = 3
PAIR = 2 * NODES
PAIRS_PER_CHUNK = 4
CHUNK = PAIRS_PER_CHUNK * PAIR
CHUNKS = GRAPHS * NODES // CHUNK
SLOTS = 4
SIDE = PAIRS_PER_CHUNK * 2 * NODES

ROW = 3 * HIDDEN
TABLE_TILE = 256
TABLE_SLOTS = 7
TABLE_TILES = -(-VOCAB // TABLE_TILE)
TABLE_ROWS = TABLE_TILES * TABLE_TILE
assert TABLE_TILES % TABLE_SLOTS == 0 and CHUNKS % SLOTS == 0

B_IAH, B_OAH, B_IH, B_HH, N_BIASES = 0, 1, 2, 5, 8


def is_first(r):
    return isinstance(r, int) and r == 0


def over_rounds(engine, rounds, slots, step):
    for s in range(slots):
        step(0, s)
    with engine.Fori(1, rounds - 1) as i:
        for s in range(slots):
            step(i, s)
    for s in range(slots):
        step(rounds - 1, s)


def later(r, s, ahead, slots):
    return r + (s + ahead) // slots, (s + ahead) % slots


def build(nc, adjacency, items, emb, w_io, w_ih, w_hh, b_io, biases, identity, out):
    f32, f32r, i32 = mybir.dt.float32, mybir.dt.float32r, mybir.dt.int32
    ALU, ACT = mybir.AluOpType, mybir.ActivationFunctionType

    with ExitStack() as ctx:
        def sbuf(name, shape, dtype=f32):
            return ctx.enter_context(nc.sbuf_tensor(name, shape, dtype))

        def psum(name):
            return ctx.enter_context(nc.psum_tensor(name, [128, 512], f32))

        def sem(name):
            return ctx.enter_context(nc.semaphore(name))

        table = nc.dram_tensor("table", [TABLE_ROWS, ROW], f32, kind="Internal").ap()

        ident = sbuf("ident", [128, 128])
        w_io_sb = sbuf("w_io_sb", [HIDDEN, 2 * HIDDEN])
        b_io_sb = sbuf("b_io_sb", [128, 2, 2 * HIDDEN])
        w_all = sbuf("w_all", [HIDDEN, 3, GATES * HIDDEN])
        w_high = sbuf("w_high", [HIDDEN, 3, GATES * HIDDEN], f32r)
        w_low = sbuf("w_low", [HIDDEN, 3, GATES * HIDDEN], f32r)
        bias = sbuf("bias", [128, N_BIASES])
        bias_ri = sbuf("bias_ri", [128, 2])
        n_pairs = GRAPHS // 2
        item = sbuf("item", [PAIR, n_pairs], i32)
        wrapped = sbuf("wrapped", [PAIR, n_pairs])
        clamped = sbuf("clamped", [PAIR, n_pairs])
        index = sbuf("index", [PAIR, n_pairs], i32)
        chunk_index = sbuf("chunk_index", [PAIR, SLOTS, PAIRS_PER_CHUNK], i32)
        row_tile = sbuf("row_tile", [128, TABLE_SLOTS, 2, ROW])
        emb_t = sbuf("emb_t", [HIDDEN, TABLE_SLOTS, 2, 128])
        rows = sbuf("rows", [PAIR, SLOTS, PAIRS_PER_CHUNK, ROW])
        adj = sbuf("adj", [PAIR, SLOTS, 2, SIDE])
        x_high = sbuf("x_high", [HIDDEN, SLOTS, 3, CHUNK], f32r)
        x_low = sbuf("x_low", [HIDDEN, SLOTS, 3, CHUNK], f32r)
        hidden_t = sbuf("hidden_t", [HIDDEN, SLOTS, CHUNK])
        reset = sbuf("reset", [HIDDEN, SLOTS, CHUNK])
        inputg = sbuf("inputg", [HIDDEN, SLOTS, CHUNK])
        gated = sbuf("gated", [HIDDEN, SLOTS, CHUNK])
        new_arg = sbuf("new_arg", [HIDDEN, SLOTS, CHUNK])
        newg = sbuf("newg", [HIDDEN, SLOTS, CHUNK])
        diff = sbuf("diff", [HIDDEN, SLOTS, CHUNK])
        scaled = sbuf("scaled", [HIDDEN, SLOTS, CHUNK])
        result = sbuf("result", [HIDDEN, SLOTS, CHUNK])

        banks = [psum(f"bank{n}") for n in range(TABLE_SLOTS)]
        agg_in, agg_out, hid_ps, reset_ps, input_ps, hidnew_ps, new_ps = banks

        ident_loaded = sem("ident_loaded")
        linear_loaded = sem("linear_loaded")
        items_loaded = sem("items_loaded")
        gates_loaded = sem("gates_loaded")
        emb_loaded = [sem(f"emb_loaded{s}") for s in range(TABLE_SLOTS)]
        emb_transposed = sem("emb_transposed")
        emb_t_copied = sem("emb_t_copied")
        linear_done = sem("linear_done")
        row_ready = sem("row_ready")
        row_stored = [sem(f"row_stored{s}") for s in range(TABLE_SLOTS)]
        wrap_ready = sem("wrap_ready")
        clamp_ready = sem("clamp_ready")
        index_ready = sem("index_ready")
        chunk_index_ready = sem("chunk_index_ready")
        gathers_begun = sem("gathers_begun")
        adj_zeroed = sem("adj_zeroed")
        w_high_ready = sem("w_high_ready")
        w_ready = sem("w_ready")
        bias_ready = sem("bias_ready")
        rows_loaded = [sem(f"rows_loaded{s}") for s in range(SLOTS)]
        adj_loaded = [sem(f"adj_loaded{s}") for s in range(SLOTS)]
        in_aggregated = sem("in_aggregated")
        out_aggregated = sem("out_aggregated")
        hidden_turned = sem("hidden_turned")
        in_high_ready = sem("in_high_ready")
        out_high_ready = sem("out_high_ready")
        hidden_copied = sem("hidden_copied")
        hidden_high_ready = sem("hidden_high_ready")
        split_done = sem("split_done")
        reset_summed = sem("reset_summed")
        input_summed = sem("input_summed")
        hidnew_summed = sem("hidnew_summed")
        new_summed = sem("new_summed")
        reset_ready = sem("reset_ready")
        input_ready = sem("input_ready")
        gated_ready = sem("gated_ready")
        new_arg_ready = sem("new_arg_ready")
        new_ready = sem("new_ready")
        diff_ready = sem("diff_ready")
        scaled_ready = sem("scaled_ready")
        result_ready = sem("result_ready")
        result_stored = [sem(f"result_stored{s}") for s in range(SLOTS)]

        TABLE_ROUNDS = TABLE_TILES // TABLE_SLOTS
        ROUNDS = CHUNKS // SLOTS

        emb_v = emb.rearrange("(t p r) h -> t p r h", p=128, r=2)
        table_v = table.rearrange("(t p r) h -> t p r h", p=128, r=2)

        block = ctx.enter_context(nc.Block())

        @block.sync
        def _(sp):
            def load_emb(r, s):
                if not is_first(r):
                    sp.wait_ge(row_stored[s], 16 * r)
                sp.dma_start(row_tile[:, s, :, 2 * HIDDEN:ROW],
                             emb_v[r * TABLE_SLOTS + s]).then_inc(emb_loaded[s], 16)

            sp.dma_start(ident[:, :], identity).then_inc(ident_loaded, 16)
            load_emb(0, 0)
            sp.dma_start(w_io_sb[:, :], w_io).then_inc(linear_loaded, 16)
            load_emb(0, 1)
            for n in range(2):
                sp.dma_start(b_io_sb[:, n, :], b_io.partition_broadcast(128)).then_inc(linear_loaded, 16)
            for s in range(2, TABLE_SLOTS):
                load_emb(0, s)

            with sp.Fori(1, TABLE_ROUNDS) as r:
                for s in range(TABLE_SLOTS):
                    load_emb(r, s)

            def load_adj(r, s):
                for g in range(2):
                    sp.dma_start(adj[g * NODES:(g + 1) * NODES, s, g, :],
                                 adjacency[r * SLOTS + s, g]).then_inc(adj_loaded[s], 16)

            sp.wait_ge(adj_zeroed, 1)
            sp.wait_ge(row_ready, TABLE_TILES)
            for s in range(SLOTS):
                load_adj(0, s)

            with sp.Fori(1, ROUNDS) as r:
                for s in range(SLOTS):
                    sp.wait_ge(out_aggregated, (r - 1) * SLOTS + s + 1)
                    load_adj(r, s)

        @block.gpsimd
        def _(pool):
            pool.dma_start(item[:, :], items).then_inc(items_loaded, 16)
            pool.dma_start(bias[:, :], biases).then_inc(gates_loaded, 16)
            for n in range(2):
                pool.dma_start(w_all[:, n, :], w_ih[n, :, :]).then_inc(gates_loaded, 16)
            pool.dma_start(w_all[:, 2, :], w_hh).then_inc(gates_loaded, 16)
            pool.memset(adj[:, :, :, :], 0.0).then_inc(adj_zeroed, 1)
            pool.wait_ge(index_ready, 1)
            for s in range(TABLE_SLOTS):
                pool.wait_ge(row_stored[s], 16 * TABLE_ROUNDS)

            def step(r, s):
                t = r * SLOTS + s
                if not is_first(r):
                    pool.wait_ge(hidden_turned, t - SLOTS + 1)
                pool.tensor_copy(chunk_index[:, s, :], index[:, bass.ds(t * PAIRS_PER_CHUNK, PAIRS_PER_CHUNK)])\
                    .then_inc(chunk_index_ready, 1)
                pool.wait_ge(chunk_index_ready, t + 1)
                pool.sem_inc(gathers_begun, 1)
                for q in range(PAIRS_PER_CHUNK):
                    pool.indirect_dma_start(
                        out=rows[:, s, q, :], out_offset=None, in_=table,
                        in_offset=bass.IndirectOffsetOnAxis(ap=chunk_index[:, s, q:q + 1], axis=0),
                    ).then_inc(rows_loaded[s], 16)

            over_rounds(pool, ROUNDS, SLOTS, step)

        @block.tensor
        def _(pe):
            pe.wait_ge(ident_loaded, 16)

            def linear(r, s):
                if is_first(r) and s == 0:
                    pe.wait_ge(linear_loaded, 48)
                pe.wait_ge(emb_t_copied, r * TABLE_SLOTS + s + 1)
                for n in range(2):
                    last = nc.tensor.matmul(banks[s][:, n * 2 * HIDDEN:(n + 1) * 2 * HIDDEN],
                                            emb_t[:, s, n, :], w_io_sb[:, :], start=True, stop=True)
                last.then_inc(linear_done, 1)

            def table_step(r, s):
                t = r * TABLE_SLOTS + s
                pe.wait_ge(emb_loaded[s], 16 * (r + 1))
                if not is_first(r):
                    pe.wait_ge(row_ready, t - TABLE_SLOTS + 1)
                for n in range(2):
                    last = nc.tensor.transpose(banks[s][:, n * 128:(n + 1) * 128],
                                               row_tile[:, s, n, 2 * HIDDEN:ROW], ident[:, :])
                last.then_inc(emb_transposed, 1)
                if s > 0:
                    linear(r, s - 1)
                elif not is_first(r):
                    linear(r - 1, TABLE_SLOTS - 1)

            over_rounds(pe, TABLE_ROUNDS, TABLE_SLOTS, table_step)
            linear(TABLE_ROUNDS - 1, TABLE_SLOTS - 1)

            pe.wait_ge(row_ready, TABLE_TILES)
            pe.wait_ge(w_ready, 3)

            def wait_rows(r, s):
                pe.wait_ge(rows_loaded[s], 16 * PAIRS_PER_CHUNK * (r + 1))

            def wait_adj(r, s):
                pe.wait_ge(adj_loaded[s], 2 * 16 * (r + 1))

            def wait_split(r, s):
                pe.wait_ge(split_done, 3 * (r * SLOTS + s))

            def aggregate(r, s):
                for n, (bank, done) in enumerate(((agg_in, in_aggregated), (agg_out, out_aggregated))):
                    for q in range(PAIRS_PER_CHUNK):
                        at = (2 * q + n) * NODES
                        last = nc.tensor.matmul(bank[:, q * PAIR:(q + 1) * PAIR],
                                                rows[:, s, q, n * HIDDEN:(n + 1) * HIDDEN],
                                                adj[:, s, :, at:at + NODES], start=True, stop=True)
                    last.then_inc(done, 1)
                for q in range(PAIRS_PER_CHUNK):
                    last = nc.tensor.transpose(hid_ps[:, q * PAIR:(q + 1) * PAIR],
                                               rows[:, s, q, 2 * HIDDEN:ROW], ident[0:PAIR, 0:PAIR])
                last.then_inc(hidden_turned, 1)

            def gate_sum(bank, gate, sources, s, done, ahead=None):
                cols = slice(gate * HIDDEN, (gate + 1) * HIDDEN)
                terms = [(w, x, n) for n in sources
                         for w, x in ((w_high, x_high), (w_high, x_low), (w_low, x_high))]
                for k, (w, x, n) in enumerate(terms):
                    if ahead is not None and 1 <= k <= 3:
                        (wait_rows, wait_adj, wait_split)[k - 1](*ahead)
                    last = nc.tensor.matmul(bank[:, 0:CHUNK], w[:, n, cols], x[:, s, n, :],
                                            start=(k == 0), stop=(k == len(terms) - 1))
                last.then_inc(done, 1)

            wait_rows(0, 0)
            wait_adj(0, 0)
            aggregate(0, 0)
            wait_rows(0, 1)
            wait_adj(0, 1)
            wait_split(0, 1)

            def step(r, s):
                t = r * SLOTS + s
                ahead = later(r, s, 1, SLOTS)
                if isinstance(r, int) and ahead[0] >= ROUNDS:
                    pe.wait_ge(split_done, 3 * CHUNKS)
                else:
                    aggregate(*ahead)
                first = isinstance(t, int) and t == 0
                if not first:
                    pe.wait_ge(reset_ready, t)
                gate_sum(reset_ps, 0, (0, 1, 2), s, reset_summed)
                if not first:
                    pe.wait_ge(input_ready, t)
                gate_sum(input_ps, 1, (0, 1, 2), s, input_summed)
                if not first:
                    pe.wait_ge(gated_ready, t)
                gate_sum(hidnew_ps, 2, (2,), s, hidnew_summed)
                if not first:
                    pe.wait_ge(new_arg_ready, t)
                after = later(r, s, 2, SLOTS)
                if isinstance(r, int) and after[0] >= ROUNDS:
                    after = None
                gate_sum(new_ps, 2, (0, 1), s, new_summed, after)

            over_rounds(pe, ROUNDS, SLOTS, step)

        @block.scalar
        def _(act):
            def store_rows(r, s):
                act.wait_ge(row_ready, r * TABLE_SLOTS + s + 1)
                act.dma_start(table_v[r * TABLE_SLOTS + s], row_tile[:, s, :, :]).then_inc(row_stored[s], 16)

            def table_step(r, s):
                act.wait_ge(emb_transposed, r * TABLE_SLOTS + s + 1)
                nc.scalar.activation(emb_t[:, s, :, :], banks[s][:, 0:256].rearrange("p (r v) -> p r v", r=2),
                                     ACT.Copy).then_inc(emb_t_copied, 1)
                if s > 0:
                    store_rows(r, s - 1)
                elif not is_first(r):
                    store_rows(r - 1, TABLE_SLOTS - 1)

            over_rounds(act, TABLE_ROUNDS, TABLE_SLOTS, table_step)
            store_rows(TABLE_ROUNDS - 1, TABLE_SLOTS - 1)

            act.wait_ge(gates_loaded, 64)
            for n in range(3):
                nc.scalar.activation(w_high[:, n, :], w_all[:, n, :], ACT.Copy).then_inc(w_high_ready, 1)
            act.wait_ge(bias_ready, 1)

            def split(r, s):
                t = r * SLOTS + s
                for n, (bank, done, ready, b) in enumerate((
                        (agg_in, in_aggregated, in_high_ready, B_IAH),
                        (agg_out, out_aggregated, out_high_ready, B_OAH))):
                    act.wait_ge(done, t + 1)
                    nc.scalar.activation(x_high[:, s, n, :], bank[:, 0:CHUNK], ACT.Identity,
                                         bias=bias[:, b:b + 1]).then_inc(ready, 1)
                act.wait_ge(hidden_turned, t + 1)
                if not is_first(r):
                    act.wait_ge(result_ready, t - SLOTS + 1)
                nc.scalar.activation(hidden_t[:, s, :], hid_ps[:, 0:CHUNK], ACT.Copy).then_inc(hidden_copied, 1)

            def store(r, s):
                act.wait_ge(result_ready, r * SLOTS + s + 1)
                act.dma_start(out[r * SLOTS + s], result[:, s, :]).then_inc(result_stored[s], 16)

            split(0, 0)

            def step(r, s):
                t = r * SLOTS + s
                ahead = later(r, s, 1, SLOTS)
                if not (isinstance(r, int) and ahead[0] >= ROUNDS):
                    split(*ahead)
                if s > 0:
                    store(r, s - 1)
                elif not is_first(r):
                    store(r - 1, SLOTS - 1)
                act.wait_ge(reset_summed, t + 1)
                if not is_first(r):
                    act.wait_ge(result_ready, t - SLOTS + 1)
                nc.scalar.activation(reset[:, s, :], reset_ps[:, 0:CHUNK], ACT.Sigmoid,
                                     bias=bias_ri[:, 0:1]).then_inc(reset_ready, 1)
                act.wait_ge(input_summed, t + 1)
                nc.scalar.activation(inputg[:, s, :], input_ps[:, 0:CHUNK], ACT.Sigmoid,
                                     bias=bias_ri[:, 1:2]).then_inc(input_ready, 1)
                act.wait_ge(new_arg_ready, t + 1)
                nc.scalar.activation(newg[:, s, :], new_arg[:, s, :], ACT.Tanh,
                                     bias=bias[:, B_IH + 2:B_IH + 3]).then_inc(new_ready, 1)

            over_rounds(act, ROUNDS, SLOTS, step)
            store(ROUNDS - 1, SLOTS - 1)
            for s in range(SLOTS):
                act.wait_ge(result_stored[s], 16 * ROUNDS)

        @block.vector
        def _(dve):
            dve.wait_ge(items_loaded, 16)
            nc.vector.tensor_scalar(wrapped[:, :], item[:, :], 0.0, float(VOCAB), ALU.is_lt, ALU.mult)\
                .then_inc(wrap_ready, 1)
            dve.wait_ge(wrap_ready, 1)
            nc.vector.scalar_tensor_tensor(clamped[:, :], item[:, :], float(VOCAB - 1), wrapped[:, :],
                                           ALU.min, ALU.add).then_inc(clamp_ready, 1)
            dve.wait_ge(clamp_ready, 1)
            nc.vector.tensor_scalar(index[:, :], clamped[:, :], 0.0, None, ALU.max).then_inc(index_ready, 1)
            def table_step(r, s):
                dve.wait_ge(linear_done, r * TABLE_SLOTS + s + 1)
                nc.vector.tensor_tensor(row_tile[:, s, :, 0:2 * HIDDEN],
                                        banks[s][:, :].rearrange("p (r c) -> p r c", r=2),
                                        b_io_sb[:, :, :], ALU.add).then_inc(row_ready, 1)

            dve.wait_ge(linear_loaded, 48)
            over_rounds(dve, TABLE_ROUNDS, TABLE_SLOTS, table_step)

            dve.wait_ge(gates_loaded, 64)
            nc.vector.tensor_tensor(bias_ri[:, :], bias[:, B_IH:B_IH + 2], bias[:, B_HH:B_HH + 2], ALU.add)\
                .then_inc(bias_ready, 1)
            for n in range(3):
                dve.wait_ge(w_high_ready, n + 1)
                nc.vector.tensor_tensor(w_low[:, n, :], w_all[:, n, :], w_high[:, n, :].bitcast(f32),
                                        ALU.subtract).then_inc(w_ready, 1)

            def split(r, s):
                t = r * SLOTS + s
                for n, (bank, ready, b) in enumerate(((agg_in, in_high_ready, B_IAH),
                                                      (agg_out, out_high_ready, B_OAH))):
                    dve.wait_ge(ready, t + 1)
                    nc.vector.scalar_tensor_tensor(x_low[:, s, n, :], bank[:, 0:CHUNK], bias[:, b:b + 1],
                                                   x_high[:, s, n, :].bitcast(f32), ALU.add, ALU.subtract)\
                        .then_inc(split_done, 1)
                dve.wait_ge(hidden_copied, t + 1)
                nc.vector.tensor_copy(x_high[:, s, 2, :], hidden_t[:, s, :]).then_inc(hidden_high_ready, 1)
                dve.wait_ge(hidden_high_ready, t + 1)
                nc.vector.tensor_tensor(x_low[:, s, 2, :], hidden_t[:, s, :], x_high[:, s, 2, :].bitcast(f32),
                                        ALU.subtract).then_inc(split_done, 1)

            split(0, 0)

            def step(r, s):
                t = r * SLOTS + s
                ahead = later(r, s, 1, SLOTS)
                if not (isinstance(r, int) and ahead[0] >= ROUNDS):
                    split(*ahead)
                dve.wait_ge(reset_ready, t + 1)
                dve.wait_ge(hidnew_summed, t + 1)
                nc.vector.scalar_tensor_tensor(gated[:, s, :], hidnew_ps[:, 0:CHUNK],
                                               bias[:, B_HH + 2:B_HH + 3], reset[:, s, :],
                                               ALU.add, ALU.mult).then_inc(gated_ready, 1)
                dve.wait_ge(new_summed, t + 1)
                dve.wait_ge(gated_ready, t + 1)
                nc.vector.tensor_tensor(new_arg[:, s, :], new_ps[:, 0:CHUNK], gated[:, s, :], ALU.add)\
                    .then_inc(new_arg_ready, 1)
                dve.wait_ge(new_ready, t + 1)
                nc.vector.tensor_tensor(diff[:, s, :], hidden_t[:, s, :], newg[:, s, :], ALU.subtract)\
                    .then_inc(diff_ready, 1)
                dve.wait_ge(diff_ready, t + 1)
                dve.wait_ge(input_ready, t + 1)
                nc.vector.tensor_tensor(scaled[:, s, :], diff[:, s, :], inputg[:, s, :], ALU.mult)\
                    .then_inc(scaled_ready, 1)
                dve.wait_ge(scaled_ready, t + 1)
                if not is_first(r):
                    dve.wait_ge(result_stored[s], 16 * r)
                nc.vector.tensor_tensor(result[:, s, :], scaled[:, s, :], newg[:, s, :], ALU.add)\
                    .then_inc(result_ready, 1)

            over_rounds(dve, ROUNDS, SLOTS, step)


def kernel(r_A, r_items, L0_rec_emb, L0_rec_w_in, L0_rec_b_in, L0_rec_w_out, L0_rec_b_out, L0_rec_w_ih,
           L0_rec_w_hh, L0_rec_b_ih, L0_rec_b_hh, L0_rec_b_iah, L0_rec_b_oah):
    import numpy as np
    import concourse.bacc as bacc
    from concourse.bass_utils import run_bass_kernel_spmd

    adjacency = np.asarray(r_A).reshape(CHUNKS, PAIRS_PER_CHUNK, 2, NODES, 2, NODES).transpose(0, 2, 5, 1, 4, 3)
    emb = np.zeros((TABLE_ROWS, HIDDEN), np.float32)
    emb[:VOCAB] = np.asarray(L0_rec_emb)
    arrays = {
        "adjacency": adjacency.reshape(CHUNKS, 2, NODES, SIDE),
        "items": np.asarray(r_items).reshape(GRAPHS // 2, PAIR).T,
        "emb": emb,
        "w_io": np.concatenate([np.asarray(L0_rec_w_in).T, np.asarray(L0_rec_w_out).T], axis=1),
        "w_ih": np.asarray(L0_rec_w_ih).T.reshape(2, HIDDEN, GATES * HIDDEN),
        "w_hh": np.asarray(L0_rec_w_hh).T,
        "b_io": np.concatenate([np.asarray(L0_rec_b_in), np.asarray(L0_rec_b_out)]),
        "biases": np.concatenate([np.asarray(L0_rec_b_iah)[None], np.asarray(L0_rec_b_oah)[None],
                                  np.asarray(L0_rec_b_ih).reshape(GATES, HIDDEN),
                                  np.asarray(L0_rec_b_hh).reshape(GATES, HIDDEN)]).T,
        "identity": np.eye(128, dtype=np.float32),
    }
    arrays = {name: np.ascontiguousarray(a) for name, a in arrays.items()}
    nc = bacc.Bacc("TRN2", target_bir_lowering=False, num_devices=1)
    aps = [nc.dram_tensor(name, a.shape, mybir.dt.from_np(a.dtype), kind="ExternalInput").ap()
           for name, a in arrays.items()]
    out = nc.dram_tensor("out", (CHUNKS, HIDDEN, CHUNK), mybir.dt.float32, kind="ExternalOutput").ap()
    build(nc, *aps, out)
    result = run_bass_kernel_spmd(nc, [arrays], core_ids=[0]).results[0]["out"]
    return np.ascontiguousarray(np.asarray(result).transpose(0, 2, 1)).reshape(GRAPHS, NODES, HIDDEN)
```
